# Optimizing a Trainium2 kernel written in Bass

```python
import numpy as np
import jax
import jax.numpy as jnp

def _softmax(x, axis=-1):
    return jax.nn.softmax(x, axis=axis)

def _gelu(x):
    return jax.nn.gelu(x, approximate=True)

def _silu(x):
    return jax.nn.silu(x)

def _sigmoid(x):
    return jax.nn.sigmoid(x)

def _layernorm(x, axis=-1, eps=1e-05):
    m = jnp.mean(x, axis=axis, keepdims=True)
    v = jnp.var(x, axis=axis, keepdims=True)
    return (x - m) / jnp.sqrt(v + eps)

def _scatter_add(tgt, idx, src, axis=0):
    return tgt.at[idx].add(src)

def _segment_sum(src, seg, n):
    return jax.ops.segment_sum(src, seg, n)
kernel_name = 'mk_dlrm_tower_d1_rec_r8_695d39'

def setup_inputs(seed: int=0):
    np.random.seed(seed)
    _w = jnp.asarray

    def _rec_inputs():
        import jax
        import jax.numpy as jnp
        _tk = jax.random.key(seed)
        ids = jnp.stack([jax.random.randint(jax.random.fold_in(_tk, 200 + f), (2048,), 0, v, jnp.int32) for f, v in enumerate([1000, 1250, 1250, 1000, 12500, 125000, 1250, 12500, 1250, 1000, 1250, 12500, 1000, 12500, 12500, 12500, 1000, 12500, 12500, 1000, 1250, 1000, 1000, 1000, 1250, 1000])], axis=1)
        tbl_0 = 0.05 * jax.random.normal(jax.random.fold_in(_tk, 500 + 0), (1000, 128), jnp.float32)
        tbl_1 = 0.05 * jax.random.normal(jax.random.fold_in(_tk, 500 + 1), (1250, 128), jnp.float32)
        tbl_2 = 0.05 * jax.random.normal(jax.random.fold_in(_tk, 500 + 2), (1250, 128), jnp.float32)
        tbl_3 = 0.05 * jax.random.normal(jax.random.fold_in(_tk, 500 + 3), (1000, 128), jnp.float32)
        tbl_4 = 0.05 * jax.random.normal(jax.random.fold_in(_tk, 500 + 4), (12500, 128), jnp.float32)
        tbl_5 = 0.05 * jax.random.normal(jax.random.fold_in(_tk, 500 + 5), (125000, 128), jnp.float32)
        tbl_6 = 0.05 * jax.random.normal(jax.random.fold_in(_tk, 500 + 6), (1250, 128), jnp.float32)
        tbl_7 = 0.05 * jax.random.normal(jax.random.fold_in(_tk, 500 + 7), (12500, 128), jnp.float32)
        tbl_8 = 0.05 * jax.random.normal(jax.random.fold_in(_tk, 500 + 8), (1250, 128), jnp.float32)
        tbl_9 = 0.05 * jax.random.normal(jax.random.fold_in(_tk, 500 + 9), (1000, 128), jnp.float32)
        tbl_10 = 0.05 * jax.random.normal(jax.random.fold_in(_tk, 500 + 10), (1250, 128), jnp.float32)
        tbl_11 = 0.05 * jax.random.normal(jax.random.fold_in(_tk, 500 + 11), (12500, 128), jnp.float32)
        tbl_12 = 0.05 * jax.random.normal(jax.random.fold_in(_tk, 500 + 12), (1000, 128), jnp.float32)
        tbl_13 = 0.05 * jax.random.normal(jax.random.fold_in(_tk, 500 + 13), (12500, 128), jnp.float32)
        tbl_14 = 0.05 * jax.random.normal(jax.random.fold_in(_tk, 500 + 14), (12500, 128), jnp.float32)
        tbl_15 = 0.05 * jax.random.normal(jax.random.fold_in(_tk, 500 + 15), (12500, 128), jnp.float32)
        tbl_16 = 0.05 * jax.random.normal(jax.random.fold_in(_tk, 500 + 16), (1000, 128), jnp.float32)
        tbl_17 = 0.05 * jax.random.normal(jax.random.fold_in(_tk, 500 + 17), (12500, 128), jnp.float32)
        tbl_18 = 0.05 * jax.random.normal(jax.random.fold_in(_tk, 500 + 18), (12500, 128), jnp.float32)
        tbl_19 = 0.05 * jax.random.normal(jax.random.fold_in(_tk, 500 + 19), (1000, 128), jnp.float32)
        tbl_20 = 0.05 * jax.random.normal(jax.random.fold_in(_tk, 500 + 20), (1250, 128), jnp.float32)
        tbl_21 = 0.05 * jax.random.normal(jax.random.fold_in(_tk, 500 + 21), (1000, 128), jnp.float32)
        tbl_22 = 0.05 * jax.random.normal(jax.random.fold_in(_tk, 500 + 22), (1000, 128), jnp.float32)
        tbl_23 = 0.05 * jax.random.normal(jax.random.fold_in(_tk, 500 + 23), (1000, 128), jnp.float32)
        tbl_24 = 0.05 * jax.random.normal(jax.random.fold_in(_tk, 500 + 24), (1250, 128), jnp.float32)
        tbl_25 = 0.05 * jax.random.normal(jax.random.fold_in(_tk, 500 + 25), (1000, 128), jnp.float32)
        _rk = jax.random.fold_in(_tk, 7)
        r_dense_features = -0.000520686 + 1.00062 * jax.random.normal(jax.random.fold_in(_rk, 101), (2048, 128), jnp.float32)
        W_top1 = 0.0405887 * jax.random.normal(jax.random.fold_in(_tk, 801), (607, 512), jnp.float32)
        W_top2 = 0.0441942 * jax.random.normal(jax.random.fold_in(_tk, 802), (512, 256), jnp.float32)
        W_top3 = 0.0625 * jax.random.normal(jax.random.fold_in(_tk, 803), (256, 1), jnp.float32)
        b_top1 = jnp.zeros((512,), jnp.float32)
        b_top2 = jnp.zeros((256,), jnp.float32)
        return (r_dense_features, ids, tbl_0, tbl_1, tbl_2, tbl_3, tbl_4, tbl_5, tbl_6, tbl_7, tbl_8, tbl_9, tbl_10, tbl_11, tbl_12, tbl_13, tbl_14, tbl_15, tbl_16, tbl_17, tbl_18, tbl_19, tbl_20, tbl_21, tbl_22, tbl_23, tbl_24, tbl_25, W_top1, b_top1, W_top2, b_top2, W_top3)
    r_dense_features, ids, tbl_0, tbl_1, tbl_2, tbl_3, tbl_4, tbl_5, tbl_6, tbl_7, tbl_8, tbl_9, tbl_10, tbl_11, tbl_12, tbl_13, tbl_14, tbl_15, tbl_16, tbl_17, tbl_18, tbl_19, tbl_20, tbl_21, tbl_22, tbl_23, tbl_24, tbl_25, W_top1, b_top1, W_top2, b_top2, W_top3 = _rec_inputs()

    def _L0_rec_setup():
        import jax, jax.numpy as jnp
        import numpy as np
        F = 26
        B, D = (2048, 128)
        _IU0, _IU1 = np.triu_indices(F + 1, k=1)
        _IU0 = jnp.asarray(_IU0)
        _IU1 = jnp.asarray(_IU1)
        key = jax.random.key(seed)
        k1, k2 = jax.random.split(key)
        dense_features = jax.random.normal(k1, (B, D), dtype=jnp.float32)
        sparse_features = jax.random.normal(k2, (B, F, D), dtype=jnp.float32)
        return {'dense_features': dense_features, 'sparse_features': sparse_features}
    _L0_rec_all = _L0_rec_setup()
    _L0_rec_in = {k: v for k, v in _L0_rec_all.items() if k in ()}
    del _L0_rec_all
    return {'r_dense_features': r_dense_features, 'ids': ids, 'tbl_0': tbl_0, 'tbl_1': tbl_1, 'tbl_2': tbl_2, 'tbl_3': tbl_3, 'tbl_4': tbl_4, 'tbl_5': tbl_5, 'tbl_6': tbl_6, 'tbl_7': tbl_7, 'tbl_8': tbl_8, 'tbl_9': tbl_9, 'tbl_10': tbl_10, 'tbl_11': tbl_11, 'tbl_12': tbl_12, 'tbl_13': tbl_13, 'tbl_14': tbl_14, 'tbl_15': tbl_15, 'tbl_16': tbl_16, 'tbl_17': tbl_17, 'tbl_18': tbl_18, 'tbl_19': tbl_19, 'tbl_20': tbl_20, 'tbl_21': tbl_21, 'tbl_22': tbl_22, 'tbl_23': tbl_23, 'tbl_24': tbl_24, 'tbl_25': tbl_25, 'W_top1': W_top1, 'b_top1': b_top1, 'W_top2': W_top2, 'b_top2': b_top2, 'W_top3': W_top3}

def reference(r_dense_features, ids, tbl_0, tbl_1, tbl_2, tbl_3, tbl_4, tbl_5, tbl_6, tbl_7, tbl_8, tbl_9, tbl_10, tbl_11, tbl_12, tbl_13, tbl_14, tbl_15, tbl_16, tbl_17, tbl_18, tbl_19, tbl_20, tbl_21, tbl_22, tbl_23, tbl_24, tbl_25, W_top1, b_top1, W_top2, b_top2, W_top3):
    import jax
    import jax.numpy as jnp

    def _L0_rec_ref(dense_features, sparse_features):
        import jax, jax.numpy as jnp
        import numpy as np
        F = 26
        B, D = (2048, 128)
        _IU0, _IU1 = np.triu_indices(F + 1, k=1)
        _IU0 = jnp.asarray(_IU0)
        _IU1 = jnp.asarray(_IU1)
        combined = jnp.concatenate([dense_features[:, None, :], sparse_features], axis=1)
        interactions = jnp.einsum('bfd,bgd->bfg', combined, combined)
        interactions_flat = interactions[:, _IU0, _IU1]
        return jnp.concatenate([dense_features, interactions_flat], axis=1)
    e = jnp.stack([tbl_0[ids[:, 0]], tbl_1[ids[:, 1]], tbl_2[ids[:, 2]], tbl_3[ids[:, 3]], tbl_4[ids[:, 4]], tbl_5[ids[:, 5]], tbl_6[ids[:, 6]], tbl_7[ids[:, 7]], tbl_8[ids[:, 8]], tbl_9[ids[:, 9]], tbl_10[ids[:, 10]], tbl_11[ids[:, 11]], tbl_12[ids[:, 12]], tbl_13[ids[:, 13]], tbl_14[ids[:, 14]], tbl_15[ids[:, 15]], tbl_16[ids[:, 16]], tbl_17[ids[:, 17]], tbl_18[ids[:, 18]], tbl_19[ids[:, 19]], tbl_20[ids[:, 20]], tbl_21[ids[:, 21]], tbl_22[ids[:, 22]], tbl_23[ids[:, 23]], tbl_24[ids[:, 24]], tbl_25[ids[:, 25]]], axis=1)
    z = _L0_rec_ref(r_dense_features, e)
    z = z.reshape(z.shape[0], -1)
    h = jnp.concatenate([z, r_dense_features], axis=1)
    h = jnp.maximum(h @ W_top1 + b_top1, 0.0)
    h = jnp.maximum(h @ W_top2 + b_top2, 0.0)
    y = h @ W_top3
    return y

_drawn_inputs = setup_inputs


def setup_inputs(seed=0):
    import zlib

    import numpy as np

    out = dict(_drawn_inputs(seed))
    spreads = {'b_top1': (0.0, 0.1), 'b_top2': (0.0, 0.1)}
    factors = {}
    for name, (base, spread) in spreads.items():
        noise = np.random.default_rng([zlib.crc32(name.encode()), seed]).standard_normal(out[name].shape)
        drawn = base * np.exp(spread * noise) if base else spread * noise
        out[name] = jnp.asarray(drawn.astype(out[name].dtype))
    for name, factor in factors.items():
        out[name] = (out[name] * factor).astype(out[name].dtype)
    return out
```

```python
from contextlib import ExitStack

import concourse.bass as bass
from concourse import mybir

BATCH, FIELDS, DIM = 2048, 26, 128
ROWS = FIELDS + 1
PADDED = 32
PAIRS = ROWS * (ROWS - 1) // 2
PAIR_CHUNKS = 3
CHUNK = PAIRS // PAIR_CHUNKS
SUPER = 256
SUPERS = BATCH // SUPER
HALVES = SUPER // 128
QUADS = 4
GROUPS = SUPER // QUADS
GRAM_CHUNK = 8
GRAM_CHUNKS = GROUPS // GRAM_CHUNK
HIDDEN1, HIDDEN2 = 512, 256
N1, N2 = HIDDEN1 // 128, HIDDEN2 // 128
ROW_PAIRS = (ROWS + 1) // 2
COLS_PER_BANK = 8
TURNS = (ROWS - 1 + COLS_PER_BANK - 1) // COLS_PER_BANK
FIRST_IDS = FIELDS // 2


def rows_of(pair):
    return [r for r in (2 * pair, 2 * pair + 1) if r < ROWS]


def columns_of(turn):
    return [c for c in range(turn * COLS_PER_BANK, (turn + 1) * COLS_PER_BANK) if c < ROWS - 1]


def pair_start(col):
    return col * (ROWS - 1) - col * (col - 1) // 2


def build(nc, dense, ids, tables, w1, b1, w2, b2, w3, out):
    f32, i32 = mybir.dt.float32, mybir.dt.int32
    ALU, ACT = mybir.AluOpType, mybir.ActivationFunctionType
    ctx = ExitStack()

    def sb(name, shape, dt=f32):
        return ctx.enter_context(nc.sbuf_tensor(name, shape, dt))

    def sem(name):
        return ctx.enter_context(nc.semaphore(name))

    with ctx:
        ident = sb("ident", [128, 128])
        index = sb("index", [128, FIELDS, HALVES], i32)
        gathered_rows = sb("gathered_rows", [128, ROWS, HALVES, DIM])
        x = sb("x", [DIM, GROUPS, QUADS, PADDED])
        dense_t = sb("dense_t", [DIM, SUPER])
        gram = sb("gram", [128, ROWS, GROUPS])
        pairs = sb("pairs", [GROUPS, QUADS, PAIRS])
        pairs_t = sb("pairs_t", [CHUNK, PAIR_CHUNKS, SUPER])
        w_dense = sb("w_dense", [DIM, 2, HIDDEN1])
        w_dense_sum = sb("w_dense_sum", [DIM, HIDDEN1])
        w_pairs = sb("w_pairs", [CHUNK, PAIR_CHUNKS, HIDDEN1])
        w_2 = sb("w_2", [128, N1, HIDDEN2])
        w_3 = sb("w_3", [128, N2])
        bias_1 = sb("bias_1", [128, N1])
        bias_2 = sb("bias_2", [128, N2])
        h1 = sb("h1", [128, N1, SUPER])
        h2 = sb("h2", [128, N2, SUPER])
        y = sb("y", [1, BATCH])

        ps_x = ctx.enter_context(nc.psum_tensor("ps_x", [128, 2, 512], f32))
        ps_gram = ctx.enter_context(nc.psum_tensor("ps_gram", [128, 2, GRAM_CHUNK, 128], f32))
        ps_m = ctx.enter_context(nc.psum_tensor("ps_m", [128, 2, 512], f32))

        ids_loaded = [sem(f"ids_loaded_{k}") for k in range(2)]
        dense_loaded = sem("dense_loaded")
        gathered = [sem(f"gathered_{f}") for f in range(FIELDS)]
        weights_loaded = sem("weights_loaded")
        w_summed = sem("w_summed")
        cleared = sem("cleared")
        ident_ready = sem("ident_ready")
        x_turned = sem("x_turned")
        x_stored = [sem("x_stored_act"), sem("x_stored_dve")]
        gram_ready = sem("gram_ready")
        gram_stored = [sem("gram_stored_act"), sem("gram_stored_dve")]
        cols_turned = sem("cols_turned")
        cols_stored = sem("cols_stored")
        pairs_turned = sem("pairs_turned")
        pairs_stored = [sem("pairs_stored_act"), sem("pairs_stored_dve")]
        l1_ready, l2_ready, l3_ready = sem("l1_ready"), sem("l2_ready"), sem("l3_ready")
        h1_stored = [sem("h1_stored_act"), sem("h1_stored_dve")]
        h2_stored = [sem("h2_stored_act"), sem("h2_stored_dve")]
        y_stored = sem("y_stored")
        y_sent = sem("y_sent")

        PER_ENGINE = ROW_PAIRS // 2

        block = ctx.enter_context(nc.Block())

        @block.sync
        def _(sp):
            def load_ids(part, at):
                lo, hi = (0, FIRST_IDS) if part == 0 else (FIRST_IDS, FIELDS)
                sp.dma_start(index[:, lo:hi, :],
                             ids[:, lo:hi, bass.ds(at, HALVES)]).then_inc(ids_loaded[part], 16)

            def load_dense(at):
                sp.dma_start(gathered_rows[:, 0, :, :],
                             dense[:, bass.ds(at, HALVES), :]).then_inc(dense_loaded, 16)

            load_ids(0, 0)
            load_ids(1, 0)
            load_dense(0)
            for dst, src in (
                (w_dense[:, 0, :], w1[0:DIM, :]),
                (w_dense[:, 1, :], w1[DIM + PAIRS:, :]),
                (w_pairs[:, :, :], w1[DIM:DIM + PAIRS, :].rearrange("(c p) n -> p c n", p=CHUNK)),
                (w_2[:, :, :], w2.rearrange("(c p) n -> p c n", p=128)),
                (w_3[:, :], w3), (bias_1[:, :], b1), (bias_2[:, :], b2),
            ):
                sp.dma_start(dst, src).then_inc(weights_loaded, 16)

            with sp.Fori(0, SUPERS - 1) as i:
                sp.wait_ge(x_turned, i * ROW_PAIRS + 1)
                sp.nop(nofuse=True)
                load_dense((i + 1) * HALVES)
                for f in range(FIRST_IDS):
                    sp.wait_ge(gathered[f], (i + 1) * 32)
                sp.nop(nofuse=True)
                load_ids(0, (i + 1) * HALVES)
                for f in range(FIRST_IDS, FIELDS):
                    sp.wait_ge(gathered[f], (i + 1) * 32)
                sp.nop(nofuse=True)
                load_ids(1, (i + 1) * HALVES)
            sp.wait_ge(y_stored, SUPERS + 1)
            sp.dma_start(out, y[:, :]).then_inc(y_sent, 16)
            sp.wait_ge(y_sent, 16)

        @block.gpsimd
        def _(pool):
            pool.memset(ident[:, :], 0.0).then_inc(cleared, 1)
            pool.wait_ge(cleared, 1)
            pool.affine_select(out=ident[:, :], in_=ident[:, :], compare_op=ALU.not_equal, fill=1.0,
                               base=0, pattern=[[-1, 128]], channel_multiplier=1).then_inc(ident_ready, 1)

            def gather(i, first):
                for f in range(FIELDS):
                    if f == 0:
                        pool.wait_ge(ids_loaded[0], (i + 1) * 16)
                        pool.nop(nofuse=True)
                    if f == FIRST_IDS:
                        pool.wait_ge(ids_loaded[1], (i + 1) * 16)
                        pool.nop(nofuse=True)
                    if not first:
                        pool.wait_ge(x_turned, i * ROW_PAIRS + ((f + 1) // 2 + 1 - ROW_PAIRS))
                        pool.nop(nofuse=True)
                    for half in range(HALVES):
                        pool.indirect_dma_start(
                            gathered_rows[:, f + 1, half, :], None, tables[f],
                            bass.IndirectOffsetOnAxis(ap=index[:, f, half:half + 1], axis=0),
                        ).then_inc(gathered[f], 16)

            gather(0, True)
            with pool.Fori(1, SUPERS) as i:
                gather(i, False)

        def source(p):
            n = len(rows_of(p))
            return ps_x[:, p % 2, 0:n * SUPER].rearrange("d (r s j) -> d r s j", r=n, s=QUADS)

        def target(p):
            r = rows_of(p)
            return x[:, :, :, r[0]:r[-1] + 1].rearrange("d j s r -> d r s j")

        def gram_copy(c, s):
            src = ps_gram[PADDED * s:PADDED * s + ROWS, c % 2, :, s * ROWS:(s + 1) * ROWS]
            dst = gram[PADDED * s:PADDED * s + ROWS, :, c * GRAM_CHUNK:(c + 1) * GRAM_CHUNK]
            return dst.rearrange("g f j -> g j f"), src

        @block.scalar
        def _(act):
            act.memzero(y[:, :]).then_inc(y_stored, 1)
            act.wait_ge(weights_loaded, 7 * 16)
            with act.Fori(0, SUPERS) as i:
                for p in range(0, ROW_PAIRS, 2):
                    act.wait_ge(x_turned, i * ROW_PAIRS + p + 1)
                    if p == 0:
                        act.activation(dense_t[:, :], ps_x[:, 0, 0:SUPER], ACT.Copy)
                    act.activation(target(p), source(p), ACT.Copy).then_inc(x_stored[0], 1)
                for c in range(GRAM_CHUNKS):
                    act.wait_ge(gram_ready, i * GRAM_CHUNKS + c + 1)
                    for s in (0, 1):
                        last = act.activation(*gram_copy(c, s), ACT.Copy)
                    last.then_inc(gram_stored[0], 1)
                act.wait_ge(pairs_turned, i * 2 + 1)
                act.activation(pairs_t[:, 0:2, :].rearrange("p c b -> p (c b)"), ps_m[0:CHUNK, 0, :],
                               ACT.Copy).then_inc(pairs_stored[0], 1)
                act.wait_ge(l1_ready, i * 2 + 1)
                for n in (0, 1):
                    last = act.activation(h1[:, n, :], ps_m[:, 0, n * SUPER:(n + 1) * SUPER], ACT.Relu,
                                          bias=bias_1[:, n:n + 1])
                last.then_inc(h1_stored[0], 1)
                act.wait_ge(l2_ready, i * 2 + 1)
                act.activation(h2[:, 0, :], ps_m[:, 0, 0:SUPER], ACT.Relu,
                               bias=bias_2[:, 0:1]).then_inc(h2_stored[0], 1)
                act.wait_ge(l3_ready, i + 1)
                act.activation(y[:, bass.ds(i * SUPER, SUPER)], ps_m[0:1, 0, 0:SUPER], ACT.Copy).then_inc(y_stored, 1)

        @block.vector
        def _(dve):
            dve.memset(x[:, :, :, ROWS:PADDED], 0.0).then_inc(w_summed, 1)
            dve.memset(gram[:, :, :], 0.0).then_inc(w_summed, 1)
            dve.wait_ge(weights_loaded, 7 * 16)
            dve.tensor_tensor(w_dense_sum[:, :], w_dense[:, 0, :], w_dense[:, 1, :],
                              ALU.add).then_inc(w_summed, 1)
            dve.wait_ge(w_summed, 3)
            with dve.Fori(0, SUPERS) as i:
                for p in range(1, ROW_PAIRS, 2):
                    dve.wait_ge(x_turned, i * ROW_PAIRS + p + 1)
                    dve.tensor_copy(target(p), source(p)).then_inc(x_stored[1], 1)
                for c in range(GRAM_CHUNKS):
                    dve.wait_ge(gram_ready, i * GRAM_CHUNKS + c + 1)
                    for s in (2, 3):
                        last = dve.tensor_copy(*gram_copy(c, s))
                    last.then_inc(gram_stored[1], 1)
                for t in range(TURNS):
                    dve.wait_ge(cols_turned, i * TURNS + t + 1)
                    for k, f in enumerate(columns_of(t)):
                        n = ROWS - 1 - f
                        at = (k % 2) * GROUPS
                        src = ps_m[at:at + GROUPS, t % 2, (k // 2) * 128:(k // 2 + 1) * 128]
                        src = src.rearrange("j (s g) -> j s g", s=QUADS)
                        last = dve.tensor_copy(pairs[:, :, pair_start(f):pair_start(f) + n], src[:, :, f + 1:ROWS])
                    last.then_inc(cols_stored, 1)
                dve.wait_ge(pairs_turned, i * 2 + 2)
                dve.tensor_copy(pairs_t[:, 2, :], ps_m[0:CHUNK, 1, 0:SUPER]).then_inc(pairs_stored[1], 1)
                dve.wait_ge(l1_ready, i * 2 + 2)
                for n in (2, 3):
                    last = dve.tensor_scalar(h1[:, n, :], ps_m[:, 1, (n - 2) * SUPER:(n - 1) * SUPER],
                                             bias_1[:, n:n + 1], 0.0, ALU.add, ALU.max)
                last.then_inc(h1_stored[1], 1)
                dve.wait_ge(l2_ready, i * 2 + 2)
                dve.tensor_scalar(h2[:, 1, :], ps_m[:, 1, 0:SUPER], bias_2[:, 1:2], 0.0,
                                  ALU.add, ALU.max).then_inc(h2_stored[1], 1)

        @block.tensor
        def _(pe):
            pe.wait_ge(ident_ready, 1)
            pe.wait_ge(w_summed, 3)
            with pe.Fori(0, SUPERS) as i:
                for p in range(ROW_PAIRS):
                    if p >= 2:
                        pe.wait_ge(x_stored[p % 2], i * PER_ENGINE + (p - 2) // 2 + 1)
                    for k, r in enumerate(rows_of(p)):
                        if r == 0:
                            pe.wait_ge(dense_loaded, (i + 1) * 16)
                        else:
                            pe.wait_ge(gathered[r - 1], (i + 1) * 32)
                        for half in range(HALVES):
                            at = k * SUPER + half * 128
                            last = pe.transpose(ps_x[:, p % 2, at:at + 128], gathered_rows[:, r, half, :], ident[:, :])
                    last.then_inc(x_turned, 1)
                pe.wait_ge(x_stored[0], (i + 1) * PER_ENGINE)
                pe.wait_ge(x_stored[1], (i + 1) * PER_ENGINE)
                for c in range(GRAM_CHUNKS):
                    if c >= 2:
                        pe.wait_ge(gram_stored[0], i * GRAM_CHUNKS + c - 1)
                        pe.wait_ge(gram_stored[1], i * GRAM_CHUNKS + c - 1)
                    for q in range(GRAM_CHUNK):
                        j = c * GRAM_CHUNK + q
                        last = pe.matmul(ps_gram[:, c % 2, q, 0:QUADS * ROWS],
                                         x[:, j, :, :].rearrange("d s r -> d (s r)"), x[:, j, :, 0:ROWS],
                                         start=True, stop=True)
                    last.then_inc(gram_ready, 1)
                pe.wait_ge(gram_stored[0], (i + 1) * GRAM_CHUNKS)
                pe.wait_ge(gram_stored[1], (i + 1) * GRAM_CHUNKS)
                pe.wait_ge(y_stored, i + 1)
                for t in range(TURNS):
                    if t >= 2:
                        pe.wait_ge(cols_stored, i * TURNS + t - 1)
                    if t < 2:
                        pe.nop(nofuse=True)
                    for k, f in enumerate(columns_of(t)[::2]):
                        last = pe.transpose(ps_m[:, t % 2, k * 128:(k + 1) * 128],
                                            gram[:, f:f + 2, :].rearrange("q f j -> q (f j)"), ident[:, :])
                    last.then_inc(cols_turned, 1)
                pe.wait_ge(cols_stored, (i + 1) * TURNS)
                pe.nop(nofuse=True)
                for c in range(PAIR_CHUNKS):
                    for s in range(QUADS):
                        at = (c % 2) * SUPER + s * GROUPS
                        last = pe.transpose(ps_m[0:CHUNK, c // 2, at:at + GROUPS],
                                            pairs[:, s, c * CHUNK:(c + 1) * CHUNK], ident[0:GROUPS, 0:GROUPS])
                    if c >= 1:
                        last.then_inc(pairs_turned, 1)
                pe.wait_ge(pairs_stored[0], i + 1)
                pe.wait_ge(pairs_stored[1], i + 1)
                for n in range(N1):
                    o = ps_m[:, n // 2, (n % 2) * SUPER:(n % 2 + 1) * SUPER]
                    w = slice(n * 128, (n + 1) * 128)
                    pe.matmul(o, w_dense_sum[:, w], dense_t[:, :], start=True, stop=False)
                    for c in range(PAIR_CHUNKS):
                        last = pe.matmul(o, w_pairs[:, c, w], pairs_t[:, c, :], start=False, stop=c == PAIR_CHUNKS - 1)
                    if n % 2:
                        last.then_inc(l1_ready, 1)
                pe.wait_ge(h1_stored[0], i + 1)
                pe.wait_ge(h1_stored[1], i + 1)
                for m in range(N2):
                    for n in range(N1):
                        last = pe.matmul(ps_m[:, m, 0:SUPER], w_2[:, n, m * 128:(m + 1) * 128], h1[:, n, :],
                                         start=n == 0, stop=n == N1 - 1)
                    last.then_inc(l2_ready, 1)
                pe.wait_ge(h2_stored[0], i + 1)
                pe.wait_ge(h2_stored[1], i + 1)
                for m in range(N2):
                    last = pe.matmul(ps_m[0:1, 0, 0:SUPER], w_3[:, m:m + 1], h2[:, m, :],
                                     start=m == 0, stop=m == N2 - 1)
                last.then_inc(l3_ready, 1)


def kernel(**inputs):
    import numpy as np
    import concourse.bacc as bacc
    from concourse.bass_utils import run_bass_kernel_spmd

    nc = bacc.Bacc("TRN2", target_bir_lowering=False, num_devices=1)
    arrays = {}

    def given(name, array):
        a = np.ascontiguousarray(array)
        arrays[name] = a
        return nc.dram_tensor(name, a.shape, mybir.dt.from_np(a.dtype), kind="ExternalInput").ap()

    def tiled(name, array):
        a = np.asarray(array)
        return given(name, a.reshape(-1, 128, a.shape[-1]).transpose(1, 0, 2))

    dense = tiled("dense_dram", inputs["r_dense_features"])
    ids = given("ids_dram", np.asarray(inputs["ids"]).reshape(-1, 128, FIELDS).transpose(1, 2, 0))
    tables = [given(f"tbl_{f}_dram", inputs[f"tbl_{f}"]) for f in range(FIELDS)]
    w1, w2 = given("w1_dram", inputs["W_top1"]), given("w2_dram", inputs["W_top2"])
    w3 = given("w3_dram", np.asarray(inputs["W_top3"]).reshape(N2, 128).T)
    b1 = given("b1_dram", np.asarray(inputs["b_top1"]).reshape(N1, 128).T)
    b2 = given("b2_dram", np.asarray(inputs["b_top2"]).reshape(N2, 128).T)
    out = nc.dram_tensor("y_dram", (1, BATCH), mybir.dt.float32, kind="ExternalOutput").ap()
    build(nc, dense, ids, tables, w1, b1, w2, b2, w3, out)
    result = run_bass_kernel_spmd(nc, [arrays], core_ids=[0])
    return result.results[0]["y_dram"].reshape(BATCH, 1)
```

```python
from contextlib import ExitStack

import concourse.bass as bass
from concourse import mybir

BATCH, FIELDS, DIM = 2048, 26, 128
HOT = [0, 3, 9, 12, 16, 19, 21]
COLD = [f for f in range(FIELDS) if f not in HOT]
HOT_SIZE = 1000
HOT_CHUNKS = 8
HOT_ROWS = HOT_SIZE // HOT_CHUNKS
HOT_BUFFERS = 4
ROWS = FIELDS + 1
PADDED = 32
PAIRS = ROWS * (ROWS - 1) // 2
PAIR_CHUNKS = 3
CHUNK = PAIRS // PAIR_CHUNKS
SUPER = 256
SUPERS = BATCH // SUPER
HALVES = SUPER // 128
QUADS = 4
GROUPS = SUPER // QUADS
GRAM_CHUNK = 8
GRAM_CHUNKS = GROUPS // GRAM_CHUNK
HIDDEN1, HIDDEN2 = 512, 256
N1, N2 = HIDDEN1 // 128, HIDDEN2 // 128
COLS_PER_BANK = 8
TURNS = (ROWS - 1 + COLS_PER_BANK - 1) // COLS_PER_BANK
FIRST_IDS = len(COLD) // 2

HOT_BANKS = [[f + 1 for f in HOT[k:k + 2]] for k in range(0, len(HOT), 2)]
COLD_ROWS = [0] + [f + 1 for f in COLD]
COLD_BANKS = [list(range(k, min(k + 2, len(COLD_ROWS)))) for k in range(0, len(COLD_ROWS), 2)]
N_HOT, N_COLD = len(HOT_BANKS), len(COLD_BANKS)
ACT_STORES = N_HOT + N_COLD // 2
DVE_STORES = N_COLD // 2
X_BANKS = 2
COLD_ROTATION = X_BANKS + 4


def columns_of(turn):
    return [c for c in range(turn * COLS_PER_BANK, (turn + 1) * COLS_PER_BANK) if c < ROWS - 1]


def pair_start(col):
    return col * (ROWS - 1) - col * (col - 1) // 2


def build(nc, dense, ids, hot_ids, tables, w1, b1, w2, b2, w3, out):
    f32, f32r, i32 = mybir.dt.float32, mybir.dt.float32r, mybir.dt.int32
    ALU, ACT = mybir.AluOpType, mybir.ActivationFunctionType
    ctx = ExitStack()

    def sb(name, shape, dt=f32):
        return ctx.enter_context(nc.sbuf_tensor(name, shape, dt))

    def sem(name):
        return ctx.enter_context(nc.semaphore(name))

    with ctx:
        ident = sb("ident", [128, 128])
        row_number = sb("row_number", [128, HOT_CHUNKS])
        row_number_int = sb("row_number_int", [128, HOT_CHUNKS], i32)
        index = sb("index", [128, len(COLD), HALVES], i32)
        cold_rows = sb("cold_rows", [128, len(COLD_ROWS), HALVES, DIM])
        hot_index = sb("hot_index", [128, len(HOT), SUPER], i32)
        hot_hi = sb("hot_hi", [HOT_ROWS, len(HOT), HOT_CHUNKS, DIM], f32r)
        hot_lo = sb("hot_lo", [HOT_ROWS, len(HOT), HOT_CHUNKS, DIM], f32r)
        onehot = sb("onehot", [HOT_ROWS, HOT_BUFFERS, HOT_CHUNKS, SUPER], f32r)
        x = sb("x", [DIM, GROUPS, QUADS, PADDED])
        dense_t = sb("dense_t", [DIM, SUPER])
        gram = sb("gram", [128, ROWS, GROUPS])
        pairs = sb("pairs", [GROUPS, QUADS, PAIRS])
        pairs_t = sb("pairs_t", [CHUNK, PAIR_CHUNKS, SUPER])
        w_dense = sb("w_dense", [DIM, 2, HIDDEN1])
        w_dense_sum = sb("w_dense_sum", [DIM, HIDDEN1])
        w_pairs = sb("w_pairs", [CHUNK, PAIR_CHUNKS, HIDDEN1])
        w_2 = sb("w_2", [128, N1, HIDDEN2])
        w_3 = sb("w_3", [128, N2])
        bias_1 = sb("bias_1", [128, N1])
        bias_2 = sb("bias_2", [128, N2])
        h1 = sb("h1", [128, N1, SUPER])
        h2 = sb("h2", [128, N2, SUPER])
        y = sb("y", [1, BATCH])
        table_size = HOT_CHUNKS * DIM
        staged = x[0:HOT_ROWS].rearrange("p j s r -> p (j s r)").rearrange("p (t n) -> p t n", n=table_size)

        ps_x = ctx.enter_context(nc.psum_tensor("ps_x", [128, COLD_ROTATION, 512], f32))
        ps_gram = ps_x[:, X_BANKS:COLD_ROTATION, :].rearrange("p k (q n) -> p (k q) n", n=128)
        ps_m = ctx.enter_context(nc.psum_tensor("ps_m", [128, 2, 512], f32))

        ids_loaded = [sem(f"ids_loaded_{k}") for k in range(2)]
        hot_ids_loaded = sem("hot_ids_loaded")
        dense_loaded = sem("dense_loaded")
        table_loaded = [sem(f"table_loaded_{t}") for t in range(len(HOT))]
        hi_ready, lo_ready = sem("hi_ready"), sem("lo_ready")
        gathered = [sem(f"gathered_{k}") for k in range(len(COLD))]
        weights_loaded = sem("weights_loaded")
        w_summed = sem("w_summed")
        cleared = sem("cleared")
        ident_ready = sem("ident_ready")
        numbered = sem("numbered")
        row_number_ready = sem("row_number_ready")
        onehot_ready = sem("onehot_ready")
        hot_read = sem("hot_read")
        cold_turned = sem("cold_turned")
        x_stored_act, x_stored_dve = sem("x_stored_act"), sem("x_stored_dve")
        gram_ready = sem("gram_ready")
        gram_stored = sem("gram_stored")
        cols_turned = sem("cols_turned")
        cols_stored = sem("cols_stored")
        pairs_turned = sem("pairs_turned")
        pairs_stored = sem("pairs_stored")
        l1_ready, l2_ready, l3_ready = sem("l1_ready"), sem("l2_ready"), sem("l3_ready")
        h1_stored = sem("h1_stored")
        h2_stored = sem("h2_stored")
        y_stored = sem("y_stored")
        y_sent = sem("y_sent")

        block = ctx.enter_context(nc.Block())

        @block.sync
        def _(sp):
            def load_ids(part, at):
                lo, hi = (0, FIRST_IDS) if part == 0 else (FIRST_IDS, len(COLD))
                sp.dma_start(index[:, lo:hi, :],
                             ids[:, lo:hi, bass.ds(at, HALVES)]).then_inc(ids_loaded[part], 16)

            def load_dense(at):
                sp.dma_start(cold_rows[:, 0, :, :],
                             dense[:, bass.ds(at, HALVES), :]).then_inc(dense_loaded, 16)

            def load_hot_ids(at):
                src = hot_ids[bass.ds(at, 1), :].rearrange("o n -> (o n)").partition_broadcast(128)
                sp.dma_start(hot_index[:, :, :].rearrange("p t b -> p (t b)"), src).then_inc(hot_ids_loaded, 16)

            load_ids(0, 0)
            load_ids(1, 0)
            for t in range(len(HOT)):
                sp.dma_start(staged[:, t, :], tables[HOT[t]].rearrange("(p c) d -> p (c d)", c=HOT_CHUNKS),
                             ).then_inc(table_loaded[t], 16)
                if t == 0:
                    load_hot_ids(0)
            load_dense(0)
            for dst, src in (
                (w_dense[:, 0, :], w1[0:DIM, :]),
                (w_dense[:, 1, :], w1[DIM + PAIRS:, :]),
                (w_pairs[:, :, :], w1[DIM:DIM + PAIRS, :].rearrange("(c p) n -> p c n", p=CHUNK)),
                (w_2[:, :, :], w2.rearrange("(c p) n -> p c n", p=128)),
                (w_3[:, :], w3), (bias_1[:, :], b1), (bias_2[:, :], b2),
            ):
                sp.dma_start(dst, src).then_inc(weights_loaded, 16)

            with sp.Fori(0, SUPERS - 1) as i:
                sp.wait_ge(onehot_ready, (i + 1) * len(HOT))
                sp.nop(nofuse=True)
                load_hot_ids(i + 1)
                sp.wait_ge(cold_turned, i * N_COLD + 1)
                sp.nop(nofuse=True)
                load_dense((i + 1) * HALVES)
                for k in range(FIRST_IDS):
                    sp.wait_ge(gathered[k], (i + 1) * 32)
                sp.nop(nofuse=True)
                load_ids(0, (i + 1) * HALVES)
                for k in range(FIRST_IDS, len(COLD)):
                    sp.wait_ge(gathered[k], (i + 1) * 32)
                sp.nop(nofuse=True)
                load_ids(1, (i + 1) * HALVES)
            sp.wait_ge(y_stored, SUPERS + 1)
            sp.dma_start(out, y[:, :]).then_inc(y_sent, 16)
            sp.wait_ge(y_sent, 16)

        @block.gpsimd
        def _(pool):
            pool.memset(ident[:, :], 0.0).then_inc(cleared, 1)
            pool.iota(row_number_int[:, :], pattern=[[1, HOT_CHUNKS]], base=0,
                      channel_multiplier=HOT_CHUNKS).then_inc(numbered, 1)
            pool.wait_ge(cleared, 1)
            pool.affine_select(out=ident[:, :], in_=ident[:, :], compare_op=ALU.not_equal, fill=1.0,
                               base=0, pattern=[[-1, 128]], channel_multiplier=1).then_inc(ident_ready, 1)

            def gather(i, first):
                for k, f in enumerate(COLD):
                    if k == 0:
                        pool.wait_ge(ids_loaded[0], (i + 1) * 16)
                        pool.nop(nofuse=True)
                    if k == FIRST_IDS:
                        pool.wait_ge(ids_loaded[1], (i + 1) * 16)
                        pool.nop(nofuse=True)
                    if not first and k % 2:
                        pool.wait_ge(cold_turned, i * N_COLD + ((k + 1) // 2 + 1 - N_COLD))
                        pool.nop(nofuse=True)
                    if not first and k == 0:
                        pool.wait_ge(cold_turned, i * N_COLD + (1 - N_COLD))
                        pool.nop(nofuse=True)
                    for half in range(HALVES):
                        pool.indirect_dma_start(
                            cold_rows[:, k + 1, half, :], None, tables[f],
                            bass.IndirectOffsetOnAxis(ap=index[:, k, half:half + 1], axis=0),
                        ).then_inc(gathered[k], 16)

            gather(0, True)
            with pool.Fori(1, SUPERS) as i:
                gather(i, False)

        def bank_to_x(bank, rows):
            n = len(rows)
            src = ps_x[:, bank, 0:n * SUPER].rearrange("d (r s j) -> d r s j", r=n, s=QUADS)
            dst = x[:, :, :, rows[0]:rows[-1] + 1:max(1, rows[-1] - rows[0])].rearrange("d j s r -> d r s j")
            return dst, src

        def cold_rows_of(b):
            return [COLD_ROWS[slot] for slot in COLD_BANKS[b]]

        def gram_copy(c, s):
            at = (c % 2) * GRAM_CHUNK
            src = ps_gram[PADDED * s:PADDED * s + ROWS, at:at + GRAM_CHUNK, s * ROWS:(s + 1) * ROWS]
            dst = gram[PADDED * s:PADDED * s + ROWS, :, c * GRAM_CHUNK:(c + 1) * GRAM_CHUNK]
            return dst.rearrange("g f j -> g j f"), src

        @block.scalar
        def _(act):
            act.memzero(y[:, :]).then_inc(y_stored, 1)
            for t in range(len(HOT)):
                act.wait_ge(table_loaded[t], 16)
                act.activation(hot_hi[:, t].rearrange("p c d -> p (c d)"), staged[:, t, :],
                               ACT.Copy).then_inc(hi_ready, 1)

            def store_hot_bank(i, a):
                act.wait_ge(hot_read, i * len(HOT) + min(2 * a + 2, len(HOT)))
                act.activation(*bank_to_x(a % X_BANKS, HOT_BANKS[a]), ACT.Copy).then_inc(x_stored_act, 1)

            def store_hot(i):
                for a in range(N_HOT):
                    store_hot_bank(i, a)

            def supertile(i, last):
                for b in range(0, N_COLD, 2):
                    act.wait_ge(cold_turned, i * N_COLD + b + 1)
                    if b == 0:
                        act.activation(dense_t[:, :], ps_x[:, 0, 0:SUPER], ACT.Copy)
                    act.activation(*bank_to_x(b % COLD_ROTATION, cold_rows_of(b)), ACT.Copy).then_inc(x_stored_act, 1)
                for c in range(GRAM_CHUNKS):
                    act.wait_ge(gram_ready, i * GRAM_CHUNKS + c + 1)
                    for s in range(QUADS):
                        done = act.activation(*gram_copy(c, s), ACT.Copy)
                    done.then_inc(gram_stored, 1)

                def hot(a):
                    if not last:
                        store_hot_bank(i + 1, a)

                hot(0)
                act.wait_ge(pairs_turned, i * 2 + 1)
                act.activation(pairs_t[:, 0:2, :].rearrange("p c b -> p (c b)"), ps_m[0:CHUNK, 0, :],
                               ACT.Copy)
                act.wait_ge(pairs_turned, i * 2 + 2)
                act.activation(pairs_t[:, 2, :], ps_m[0:CHUNK, 1, 0:SUPER], ACT.Copy).then_inc(pairs_stored, 1)
                hot(1)
                for n in range(N1):
                    if n % 2 == 0:
                        act.wait_ge(l1_ready, i * 2 + n // 2 + 1)
                    done = act.activation(h1[:, n, :], ps_m[:, n // 2, (n % 2) * SUPER:(n % 2 + 1) * SUPER],
                                          ACT.Relu, bias=bias_1[:, n:n + 1])
                done.then_inc(h1_stored, 1)
                hot(2)
                for m in range(N2):
                    act.wait_ge(l2_ready, i * 2 + m + 1)
                    done = act.activation(h2[:, m, :], ps_m[:, m, 0:SUPER], ACT.Relu, bias=bias_2[:, m:m + 1])
                done.then_inc(h2_stored, 1)
                hot(3)
                act.wait_ge(l3_ready, i + 1)
                act.activation(y[:, bass.ds(i * SUPER, SUPER)], ps_m[0:1, 0, 0:SUPER],
                               ACT.Copy).then_inc(y_stored, 1)

            act.wait_ge(lo_ready, len(HOT))
            store_hot(0)
            act.wait_ge(weights_loaded, 7 * 16)
            with act.Fori(0, SUPERS - 1) as i:
                supertile(i, False)
            supertile(SUPERS - 1, True)

        @block.vector
        def _(dve):
            for t in range(len(HOT)):
                dve.wait_ge(hi_ready, t + 1)
                dve.tensor_tensor(hot_lo[:, t].rearrange("p c d -> p (c d)"), staged[:, t, :],
                                  hot_hi[:, t].rearrange("p c d -> p (c d)").bitcast(f32),
                                  ALU.subtract).then_inc(lo_ready, 1)
                if t == 0:
                    dve.wait_ge(numbered, 1)
                    dve.tensor_copy(row_number[:, :], row_number_int[:, :]).then_inc(row_number_ready, 1)
            dve.wait_ge(lo_ready, len(HOT))
            dve.memset(x[:, :, :, ROWS:PADDED], 0.0).then_inc(w_summed, 1)
            dve.memset(gram[:, :, :], 0.0).then_inc(w_summed, 1)
            dve.wait_ge(row_number_ready, 1)

            def make_onehot(i, t, free):
                if free is not None:
                    dve.wait_ge(hot_read, free)
                for c in range(HOT_CHUNKS):
                    done = dve.tensor_scalar(onehot[:, t % HOT_BUFFERS, c, :], hot_index[0:HOT_ROWS, t, :],
                                             row_number[0:HOT_ROWS, c:c + 1], None, ALU.is_equal)
                done.then_inc(onehot_ready, 1)

            def supertile(i, last):
                for b in range(1, N_COLD, 2):
                    dve.wait_ge(cold_turned, i * N_COLD + b + 1)
                    dve.tensor_copy(*bank_to_x(b % COLD_ROTATION, cold_rows_of(b))).then_inc(x_stored_dve, 1)
                if not last:
                    dve.wait_ge(hot_ids_loaded, (i + 2) * 16)
                    for t in range(HOT_BUFFERS):
                        users = [u for u in range(len(HOT)) if u % HOT_BUFFERS == t]
                        make_onehot(i + 1, t, i * len(HOT) + users[-1] + 1)
                for t in range(TURNS):
                    dve.wait_ge(cols_turned, i * TURNS + t + 1)
                    for k, f in enumerate(columns_of(t)):
                        n = ROWS - 1 - f
                        at = (k % 2) * GROUPS
                        src = ps_m[at:at + GROUPS, t % 2, (k // 2) * 128:(k // 2 + 1) * 128]
                        src = src.rearrange("j (s g) -> j s g", s=QUADS)
                        done = dve.tensor_copy(pairs[:, :, pair_start(f):pair_start(f) + n], src[:, :, f + 1:ROWS])
                    done.then_inc(cols_stored, 1)
                if not last:
                    for t in range(HOT_BUFFERS, len(HOT)):
                        make_onehot(i + 1, t, (i + 1) * len(HOT) + (t + 1 - HOT_BUFFERS))

            dve.wait_ge(hot_ids_loaded, 16)
            for t in range(len(HOT)):
                make_onehot(0, t, t + 1 - HOT_BUFFERS if t >= HOT_BUFFERS else None)
            dve.wait_ge(weights_loaded, 7 * 16)
            dve.tensor_tensor(w_dense_sum[:, :], w_dense[:, 0, :], w_dense[:, 1, :],
                              ALU.add).then_inc(w_summed, 1)
            dve.wait_ge(w_summed, 2)
            with dve.Fori(0, SUPERS - 1) as i:
                supertile(i, False)
            supertile(SUPERS - 1, True)

        @block.tensor
        def _(pe):
            def read_hot(i, t):
                if t % 2 == 0 and t // 2 >= X_BANKS:
                    pe.wait_ge(x_stored_act, i * ACT_STORES + t // 2 - 1)
                pe.wait_ge(onehot_ready, i * len(HOT) + t + 1)
                out_ = ps_x[:, (t // 2) % 2, (t % 2) * SUPER:(t % 2 + 1) * SUPER]
                for c in range(HOT_CHUNKS):
                    for part in (hot_hi, hot_lo):
                        done = pe.matmul(out_, part[:, t, c, :], onehot[:, t % HOT_BUFFERS, c, :],
                                         start=c == 0 and part is hot_hi,
                                         stop=c == HOT_CHUNKS - 1 and part is hot_lo)
                done.then_inc(hot_read, 1)

            def supertile(i, last):
                def hot(*ts):
                    if not last:
                        for t in ts:
                            read_hot(i + 1, t)

                for b in range(N_COLD):
                    before = b - COLD_ROTATION
                    if b < X_BANKS:
                        hot_last = max(a for a in range(N_HOT) if a % X_BANKS == b)
                        pe.wait_ge(x_stored_act, i * ACT_STORES + hot_last + 1)
                    elif before >= 0 and b % 2 == 0:
                        pe.wait_ge(x_stored_act, i * ACT_STORES + N_HOT + before // 2 + 1)
                    elif before >= 0:
                        pe.wait_ge(x_stored_dve, i * DVE_STORES + before // 2 + 1)
                    for k, slot in enumerate(COLD_BANKS[b]):
                        if slot == 0:
                            pe.wait_ge(dense_loaded, (i + 1) * 16)
                        else:
                            pe.wait_ge(gathered[slot - 1], (i + 1) * 32)
                        for half in range(HALVES):
                            at = k * SUPER + half * 128
                            done = pe.transpose(ps_x[:, b % COLD_ROTATION, at:at + 128], cold_rows[:, slot, half, :], ident[:, :])
                    done.then_inc(cold_turned, 1)
                pe.wait_ge(x_stored_act, (i + 1) * ACT_STORES)
                pe.wait_ge(x_stored_dve, (i + 1) * DVE_STORES)
                for c in range(GRAM_CHUNKS):
                    if c >= 2:
                        pe.wait_ge(gram_stored, i * GRAM_CHUNKS + c - 1)
                    for q in range(GRAM_CHUNK):
                        j = c * GRAM_CHUNK + q
                        done = pe.matmul(ps_gram[:, (c % 2) * GRAM_CHUNK + q, 0:QUADS * ROWS],
                                         x[:, j, :, :].rearrange("d s r -> d (s r)"), x[:, j, :, 0:ROWS],
                                         start=True, stop=True)
                    done.then_inc(gram_ready, 1)
                hot(0)
                pe.wait_ge(gram_stored, (i + 1) * GRAM_CHUNKS)
                pe.wait_ge(y_stored, i + 1)
                for t in range(TURNS):
                    if t >= 2:
                        pe.wait_ge(cols_stored, i * TURNS + t - 1)
                    else:
                        pe.nop(nofuse=True)
                    for k, f in enumerate(columns_of(t)[::2]):
                        done = pe.transpose(ps_m[:, t % 2, k * 128:(k + 1) * 128],
                                            gram[:, f:f + 2, :].rearrange("q f j -> q (f j)"), ident[:, :])
                    done.then_inc(cols_turned, 1)
                    if t == 1:
                        hot(1, 2)
                hot(3)
                pe.wait_ge(cols_stored, (i + 1) * TURNS)
                pe.nop(nofuse=True)
                for c in range(PAIR_CHUNKS):
                    for s in range(QUADS):
                        at = (c % 2) * SUPER + s * GROUPS
                        done = pe.transpose(ps_m[0:CHUNK, c // 2, at:at + GROUPS],
                                            pairs[:, s, c * CHUNK:(c + 1) * CHUNK], ident[0:GROUPS, 0:GROUPS])
                    if c >= 1:
                        done.then_inc(pairs_turned, 1)
                hot(4)
                pe.wait_ge(pairs_stored, i + 1)
                for n in range(N1):
                    o = ps_m[:, n // 2, (n % 2) * SUPER:(n % 2 + 1) * SUPER]
                    w = slice(n * 128, (n + 1) * 128)
                    pe.matmul(o, w_dense_sum[:, w], dense_t[:, :], start=True, stop=False)
                    for c in range(PAIR_CHUNKS):
                        done = pe.matmul(o, w_pairs[:, c, w], pairs_t[:, c, :], start=False, stop=c == PAIR_CHUNKS - 1)
                    if n % 2:
                        done.then_inc(l1_ready, 1)
                hot(5)
                pe.wait_ge(h1_stored, i + 1)
                for m in range(N2):
                    for n in range(N1):
                        done = pe.matmul(ps_m[:, m, 0:SUPER], w_2[:, n, m * 128:(m + 1) * 128], h1[:, n, :],
                                         start=n == 0, stop=n == N1 - 1)
                    done.then_inc(l2_ready, 1)
                hot(*range(6, len(HOT)))
                pe.wait_ge(h2_stored, i + 1)
                for m in range(N2):
                    done = pe.matmul(ps_m[0:1, 0, 0:SUPER], w_3[:, m:m + 1], h2[:, m, :],
                                     start=m == 0, stop=m == N2 - 1)
                done.then_inc(l3_ready, 1)

            pe.wait_ge(lo_ready, len(HOT))
            for t in range(len(HOT)):
                read_hot(0, t)
            pe.wait_ge(ident_ready, 1)
            pe.wait_ge(w_summed, 3)
            with pe.Fori(0, SUPERS - 1) as i:
                supertile(i, False)
            supertile(SUPERS - 1, True)


def kernel(**inputs):
    import numpy as np
    import concourse.bacc as bacc
    from concourse.bass_utils import run_bass_kernel_spmd

    nc = bacc.Bacc("TRN2", target_bir_lowering=False, num_devices=1)
    arrays = {}

    def given(name, array):
        a = np.ascontiguousarray(array)
        arrays[name] = a
        return nc.dram_tensor(name, a.shape, mybir.dt.from_np(a.dtype), kind="ExternalInput").ap()

    dense = given("dense_dram", np.asarray(inputs["r_dense_features"]).reshape(-1, 128, DIM).transpose(1, 0, 2))
    all_ids = np.asarray(inputs["ids"])
    ids = given("ids_dram", all_ids[:, COLD].reshape(-1, 128, len(COLD)).transpose(1, 2, 0))
    hot_ids = given("hot_ids_dram", all_ids[:, HOT].reshape(SUPERS, SUPER, len(HOT))
                    .transpose(0, 2, 1).reshape(SUPERS, -1))
    tables = [given(f"tbl_{f}_dram", inputs[f"tbl_{f}"]) for f in range(FIELDS)]
    w1, w2 = given("w1_dram", inputs["W_top1"]), given("w2_dram", inputs["W_top2"])
    w3 = given("w3_dram", np.asarray(inputs["W_top3"]).reshape(N2, 128).T)
    b1 = given("b1_dram", np.asarray(inputs["b_top1"]).reshape(N1, 128).T)
    b2 = given("b2_dram", np.asarray(inputs["b_top2"]).reshape(N2, 128).T)
    out = nc.dram_tensor("y_dram", (1, BATCH), mybir.dt.float32, kind="ExternalOutput").ap()
    build(nc, dense, ids, hot_ids, tables, w1, b1, w2, b2, w3, out)
    result = run_bass_kernel_spmd(nc, [arrays], core_ids=[0])
    return result.results[0]["y_dram"].reshape(BATCH, 1)
```

```python
from contextlib import ExitStack

import concourse.bass as bass
from concourse import mybir

BATCH, FIELDS, DIM = 2048, 26, 128
HOT = [0, 3, 9, 12, 16, 19, 21]
COLD = [f for f in range(FIELDS) if f not in HOT]
HOT_SIZE = 1000
HOT_CHUNKS = 8
HOT_ROWS = HOT_SIZE // HOT_CHUNKS
HOT_BUFFERS = 4
ROWS = FIELDS + 1
PLACES = [0] + [f + 1 for f in COLD] + [f + 1 for f in HOT]
COLD_SLOTS = len(COLD)
PADDED = 32
PAIRS = ROWS * (ROWS - 1) // 2
PAIR_CHUNKS = 3
CHUNK = PAIRS // PAIR_CHUNKS
SUPER = 256
SUPERS = BATCH // SUPER
HALVES = SUPER // 128
QUADS = 4
SIDE = ROWS - 1
STATIONARY = (QUADS - 1) * PADDED + SIDE
GROUPS = SUPER // QUADS
GRAM_CHUNK = 8
GRAM_CHUNKS = GROUPS // GRAM_CHUNK
HALF_CHUNKS = GRAM_CHUNKS // HALVES
HIDDEN1, HIDDEN2 = 512, 256
N1, N2 = HIDDEN1 // 128, HIDDEN2 // 128
COLS_PER_BANK = 8
TURNS = (ROWS - 1 + COLS_PER_BANK - 1) // COLS_PER_BANK

HOT_BANKS = [list(range(k, min(k + 2, len(HOT)))) for k in range(0, len(HOT), 2)]
COLD_BANKS = [list(range(k, min(k + 4, COLD_SLOTS))) for k in range(0, COLD_SLOTS, 4)]
W2_SLOT = 11
N_HOT, N_COLD = len(HOT_BANKS), len(COLD_BANKS)
COLD_TURNS = HALVES * N_COLD
DVE_COLD = COLD_TURNS // 2
ACT_STORES = N_HOT + COLD_TURNS - DVE_COLD
X_BANKS = 2
COLD_PS = [3, 4, 2, 5, 6]
TURN_PS = [2, 3, 4, 5]
LAST_PS = [0, 1, 7, 3, 2]
LATE_BANKS = {8: 1, 9: 2}
LAST_L1_PS = [0, 6, 1, 7]


def gathers_of(bank):
    return len(COLD_BANKS[bank])


def columns_of(turn):
    return [c for c in range(turn * COLS_PER_BANK, (turn + 1) * COLS_PER_BANK) if c < ROWS - 1]


def pair_start(col):
    return col * (ROWS - 1) - col * (col - 1) // 2


def pair_order():
    order = []
    for p in range(ROWS):
        for q in range(p + 1, ROWS):
            low, high = sorted((PLACES[p], PLACES[q]))
            order.append(pair_start(low) + high - low - 1)
    return order


def build(nc, dense, ids, hot_ids, tables, w_dense, w_pairs, w_2, b1, b2, w_3, out):
    f32, f32r, i32 = mybir.dt.float32, mybir.dt.float32r, mybir.dt.int32
    ALU, ACT = mybir.AluOpType, mybir.ActivationFunctionType
    ctx = ExitStack()

    def sb(name, shape, dt=f32):
        return ctx.enter_context(nc.sbuf_tensor(name, shape, dt))

    def sem(name):
        return ctx.enter_context(nc.semaphore(name))

    with ctx:
        ident = sb("ident", [128, 128])
        row_number = sb("row_number", [128, HOT_CHUNKS])
        row_number_int = sb("row_number_int", [128, HOT_CHUNKS], i32)
        index = sb("index", [128, HALVES, COLD_SLOTS], i32)
        cold_rows = sb("cold_rows", [128, HALVES, COLD_SLOTS, DIM])
        dense_rows = sb("dense_rows", [DIM, SUPER])
        hot_index = sb("hot_index", [128, len(HOT), SUPER], i32)
        hot_hi = sb("hot_hi", [HOT_ROWS, len(HOT), HOT_CHUNKS, DIM], f32r)
        hot_lo = sb("hot_lo", [HOT_ROWS, len(HOT), HOT_CHUNKS, DIM], f32r)
        onehot = sb("onehot", [HOT_ROWS, HOT_BUFFERS, HOT_CHUNKS, SUPER], f32r)
        x = sb("x", [DIM, GROUPS, QUADS, PADDED])
        gram = sb("gram", [128, SIDE, GROUPS])
        dense_hi, dense_lo = sb("dense_hi", [DIM, SUPER], f32r), sb("dense_lo", [DIM, SUPER], f32r)
        pairs_hi = sb("pairs_hi", [CHUNK, PAIR_CHUNKS, SUPER], f32r)
        pairs_lo = sb("pairs_lo", [CHUNK, PAIR_CHUNKS, SUPER], f32r)
        hidden = sb("hidden", [128, (N1 + N2) * SUPER])
        h1_hi, h1_lo = sb("h1_hi", [128, N1, SUPER], f32r), sb("h1_lo", [128, N1, SUPER], f32r)
        wd_hi, wd_lo = sb("wd_hi", [DIM, HIDDEN1], f32r), sb("wd_lo", [DIM, HIDDEN1], f32r)
        wp_hi = sb("wp_hi", [CHUNK, PAIR_CHUNKS, HIDDEN1], f32r)
        wp_lo = sb("wp_lo", [CHUNK, PAIR_CHUNKS, HIDDEN1], f32r)
        w2_hi, w2_lo = sb("w2_hi", [128, N1, HIDDEN2], f32r), sb("w2_lo", [128, N1, HIDDEN2], f32r)
        w3_sb = sb("w3_sb", [128, N2])
        bias_1 = sb("bias_1", [128, N1])
        bias_2 = sb("bias_2", [128, N2])
        weighed = sb("weighed", [128, 2, SUPER])
        ones = sb("ones", [128, 1])
        y = sb("y", [128, BATCH // 128])
        table_size = HOT_CHUNKS * DIM
        staged = x[0:HOT_ROWS].rearrange("p j s r -> p (j s r)").rearrange("p (t n) -> p t n", n=table_size)
        wd_staged = hidden[:, 0:2 * HIDDEN1].rearrange("p (t n) -> p t n", t=2)
        wp_staged = hidden[0:CHUNK, 0:PAIR_CHUNKS * HIDDEN1].rearrange("p (c n) -> p c n", c=PAIR_CHUNKS)
        w2_staged = cold_rows[:, HALVES - 1, W2_SLOT:W2_SLOT + N1 * HIDDEN2 // DIM, :]
        w2_staged = w2_staged.rearrange("p r d -> p (r d)").rearrange("p (c n) -> p c n", c=N1)
        pairs = hidden[0:GROUPS, 0:QUADS * PAIRS].rearrange("j (s k) -> j s k", s=QUADS)
        h1 = hidden[:, 0:N1 * SUPER].rearrange("p (n b) -> p n b", n=N1)
        h2 = hidden[:, N1 * SUPER:(N1 + N2) * SUPER].rearrange("p (n b) -> p n b", n=N2)

        ps = ctx.enter_context(nc.psum_tensor("ps", [128, 8, 512], f32))
        ps_m = ps[:, 2:4, :]
        ps_gram = ps[:, 4:8, :].rearrange("p k (q n) -> p (k q) n", n=128)

        ids_loaded = [sem(f"ids_loaded_{h}") for h in range(HALVES)]
        dense_loaded = sem("dense_loaded")
        dense_placed = sem("dense_placed")
        hot_ids_loaded = sem("hot_ids_loaded")
        table_loaded = [sem(f"table_loaded_{t}") for t in range(len(HOT))]
        hi_ready, lo_ready = sem("hi_ready"), sem("lo_ready")
        gathered = [[sem(f"gathered_{h}_{b}") for b in range(N_COLD)] for h in range(HALVES)]
        small_weights_loaded = sem("small_weights_loaded")
        weights_staged = [sem(f"weights_staged_{k}") for k in range(3)]
        wd_summed = sem("wd_summed")
        weights_hi, weights_lo = sem("weights_hi"), sem("weights_lo")
        padding_cleared = sem("padding_cleared")
        cleared = sem("cleared")
        ident_ready = sem("ident_ready")
        numbered = sem("numbered")
        row_number_ready = sem("row_number_ready")
        onehot_ready = sem("onehot_ready")
        hot_read = sem("hot_read")
        cold_turned = sem("cold_turned")
        stored_act, stored_dve = sem("stored_act"), sem("stored_dve")
        dense_split = [sem("dense_split_act"), sem("dense_split_dve")]
        gram_ready = sem("gram_ready")
        gram_stored = sem("gram_stored")
        gram_stored_dve = sem("gram_stored_dve")
        cols_turned = sem("cols_turned")
        cols_stored = [sem("cols_stored_act"), sem("cols_stored_dve")]
        pairs_turned = sem("pairs_turned")
        pairs_split = [sem("pairs_split_act"), sem("pairs_split_dve")]
        l1_ready, l2_ready, l3_ready = sem("l1_ready"), sem("l2_ready"), sem("l3_ready")
        h1_stored = sem("h1_stored")
        h1_split = [sem("h1_split_act"), sem("h1_split_dve")]
        h2_stored = sem("h2_stored")
        weighed_ready = sem("weighed_ready")
        ones_ready = sem("ones_ready")
        y_stored = sem("y_stored")
        y_sent = sem("y_sent")

        def cold_stored(m):
            return m // 2 + 1, (m + 1) // 2

        block = ctx.enter_context(nc.Block())

        @block.sync
        def _(sp):
            def load_ids(h, i):
                sp.dma_start(index[:, h, :], ids[:, h, bass.ds(i, 1), :].rearrange("p o f -> p (o f)")
                             ).then_inc(ids_loaded[h], 16)

            def load_dense(i):
                sp.dma_start(dense_rows[:, :], dense[bass.ds(i, 1), :, :].rearrange("o d b -> (o d) b")
                             ).then_inc(dense_loaded, 16)

            def load_hot_ids(i):
                src = hot_ids[bass.ds(i, 1), :].rearrange("o n -> (o n)").partition_broadcast(128)
                sp.dma_start(hot_index[:, :, :].rearrange("p t b -> p (t b)"), src).then_inc(hot_ids_loaded, 16)

            load_ids(0, 0)
            for t in range(len(HOT)):
                sp.dma_start(staged[:, t, :], tables[HOT[t]].rearrange("(p c) d -> p (c d)", c=HOT_CHUNKS)
                             ).then_inc(table_loaded[t], 16)
                if t == 0:
                    load_hot_ids(0)
            load_ids(1, 0)
            load_dense(0)
            for dst, src in ((w3_sb[:, :], w_3), (bias_1[:, :], b1), (bias_2[:, :], b2)):
                sp.dma_start(dst, src).then_inc(small_weights_loaded, 16)
            sp.dma_start(w2_staged, w_2).then_inc(weights_staged[0], 16)
            sp.dma_start(wd_staged, w_dense).then_inc(weights_staged[1], 16)

            def load_next(i, first):
                for h in range(HALVES):
                    for b in range(N_COLD):
                        sp.wait_ge(gathered[h][b], (i + 1) * gathers_of(b) * 16)
                    sp.nop(nofuse=True)
                    load_ids(h, i + 1)
                    if h == 0:
                        sp.wait_ge(onehot_ready, (i + 1) * len(HOT))
                        sp.nop(nofuse=True)
                        load_hot_ids(i + 1)
                    if first and h == 0:
                        sp.wait_ge(weights_lo, 2)
                        sp.dma_start(wp_staged, w_pairs).then_inc(weights_staged[2], 16)
                    if h == 0:
                        sp.wait_ge(dense_placed, i + 1)
                        sp.wait_ge(dense_split[0], i + 1)
                        sp.wait_ge(dense_split[1], i + 1)
                        sp.nop(nofuse=True)
                        load_dense(i + 1)

            load_next(0, True)
            with sp.Fori(1, SUPERS - 1) as i:
                load_next(i, False)
            sp.wait_ge(y_stored, SUPERS + 1)
            sp.dma_start(out, y[:, :]).then_inc(y_sent, 16)
            sp.wait_ge(y_sent, 16)

        @block.gpsimd
        def _(pool):
            pool.memset(ident[:, :], 0.0).then_inc(cleared, 1)
            pool.iota(row_number_int[:, :], pattern=[[1, HOT_CHUNKS]], base=0,
                      channel_multiplier=HOT_CHUNKS).then_inc(numbered, 1)
            pool.wait_ge(cleared, 1)
            pool.affine_select(out=ident[:, :], in_=ident[:, :], compare_op=ALU.not_equal, fill=1.0,
                               base=0, pattern=[[-1, 128]], channel_multiplier=1).then_inc(ident_ready, 1)

            def gather(i, first):
                for h in range(HALVES):
                    pool.wait_ge(ids_loaded[h], (i + 1) * 16)
                    pool.nop(nofuse=True)
                    for b in range(N_COLD):
                        if not first:
                            pool.wait_ge(cold_turned, i * COLD_TURNS + (h * N_COLD + b + 1 - COLD_TURNS))
                            pool.nop(nofuse=True)
                        for slot in COLD_BANKS[b]:
                            if first and h == HALVES - 1 and slot == W2_SLOT:
                                pool.wait_ge(weights_lo, 1)
                                pool.nop(nofuse=True)
                            pool.indirect_dma_start(
                                cold_rows[:, h, slot, :], None, tables[COLD[slot]],
                                bass.IndirectOffsetOnAxis(ap=index[:, h, slot:slot + 1], axis=0),
                            ).then_inc(gathered[h][b], 16)

            gather(0, True)
            with pool.Fori(1, SUPERS) as i:
                gather(i, False)

        def cold_bank(m, last):
            return (LAST_PS if last and m >= N_COLD else COLD_PS)[m % N_COLD]

        def cold_store(m, last):
            h, b = divmod(m, N_COLD)
            slots = COLD_BANKS[b]
            src = ps[:, cold_bank(m, last), 0:len(slots) * 128].rearrange("d (r b) -> d r b", b=128)
            js = slice(h * GROUPS // HALVES, (h + 1) * GROUPS // HALVES)
            return x[:, js, :, 1 + slots[0]:2 + slots[-1]].rearrange("d j s r -> d r (j s)"), src

        def hot_store(a):
            n, first = len(HOT_BANKS[a]), 1 + COLD_SLOTS + HOT_BANKS[a][0]
            src = ps[:, a % X_BANKS, 0:n * SUPER].rearrange("d (r b) -> d r b", b=SUPER)
            return x[:, :, :, first:first + n].rearrange("d j s r -> d r (j s)"), src

        def gram_copy(c, s):
            at = (c % 2) * GRAM_CHUNK
            src = ps_gram[PADDED * s:PADDED * s + SIDE, at:at + GRAM_CHUNK, s * SIDE:(s + 1) * SIDE]
            dst = gram[PADDED * s:PADDED * s + SIDE, :, c * GRAM_CHUNK:(c + 1) * GRAM_CHUNK]
            return dst.rearrange("g f j -> g j f"), src

        def store_columns(engine, copy, i, t, odd):
            engine.wait_ge(cols_turned, i * TURNS + t + 1)
            for k, f in enumerate(columns_of(t)):
                if k % 2 == odd:
                    n = ROWS - 1 - f
                    at = odd * GROUPS
                    src = ps[at:at + GROUPS, TURN_PS[t], (k // 2) * 128:(k // 2 + 1) * 128]
                    src = src.rearrange("j (s g) -> j s g", s=QUADS)
                    done = copy(pairs[:, :, pair_start(f):pair_start(f) + n], src[:, :, f:SIDE])
            return done

        def l1_out(n, last):
            if last:
                return ps[:, LAST_L1_PS[n], 0:SUPER]
            return ps_m[:, n // 2, (n % 2) * SUPER:(n % 2 + 1) * SUPER]

        def turned_pairs(part, dst):
            chunks = [0, 1] if part == 0 else [2]
            src = ps_m[0:CHUNK, part, 0:len(chunks) * SUPER].rearrange("p (c s j) -> p c s j", c=len(chunks), s=QUADS)
            return dst[:, chunks[0]:chunks[-1] + 1, :].rearrange("p c (j s) -> p c s j", s=QUADS), src

        weights = ((w2_staged, w2_hi, w2_lo), (wd_staged[:, 0, :], wd_hi, wd_lo), (wp_staged, wp_hi, wp_lo))

        @block.scalar
        def _(act):
            def store_hot(i, a):
                act.wait_ge(hot_read, i * len(HOT) + min(2 * a + 2, len(HOT)))
                act.activation(*hot_store(a), ACT.Copy).then_inc(stored_act, 1)

            def place_dense(i):
                act.wait_ge(dense_loaded, (i + 1) * 16)
                act.activation(x[:, :, :, 0:1].rearrange("d j s r -> d (j s r)"), dense_rows[:, :],
                               ACT.Copy).then_inc(dense_placed, 1)

            def copy(dst, src):
                return act.activation(dst, src, ACT.Copy)

            def supertile(i, first, last):
                def hot(a):
                    if not last:
                        store_hot(i + 1, a)

                def store_cold(banks):
                    for m in banks:
                        if m % 2 == 0:
                            act.wait_ge(cold_turned, i * COLD_TURNS + m + 1)
                            act.activation(*cold_store(m, last), ACT.Copy).then_inc(stored_act, 1)

                store_cold(range(N_COLD))
                if first:
                    for a in range(HOT_BUFFERS // 2, N_HOT):
                        store_hot(0, a)
                    split_high(1)
                act.activation(dense_hi[:, :], dense_rows[:, :], ACT.Copy).then_inc(dense_split[0], 1)
                for h in range(HALVES):
                    if last and h == 0:
                        store_cold(m for m in range(N_COLD, COLD_TURNS) if m not in LATE_BANKS)
                    if not last and h == 1:
                        store_cold(range(N_COLD, COLD_TURNS))
                    for c in range(h * HALF_CHUNKS, (h + 1) * HALF_CHUNKS):
                        act.wait_ge(gram_ready, i * GRAM_CHUNKS + c + 1)
                        for s in range(QUADS // 2 if last else QUADS):
                            done = act.activation(*gram_copy(c, s), ACT.Copy)
                        done.then_inc(gram_stored, 1)
                        if last:
                            store_cold(m for m, after in LATE_BANKS.items() if after == c)
                    if first and h == 0:
                        split_high(2)
                if not last:
                    place_dense(i + 1)
                hot(0)
                if first:
                    act.wait_ge(weights_lo, len(weights))
                for t in range(TURNS):
                    store_columns(act, copy, i, t, 1).then_inc(cols_stored[0], 1)
                hot(1)
                for part in range(2):
                    act.wait_ge(pairs_turned, i * 2 + part + 1)
                    act.activation(*turned_pairs(part, pairs_hi), ACT.Copy).then_inc(pairs_split[0], 1)
                for n in range(N1):
                    if n % 2 == 0:
                        act.wait_ge(l1_ready, i * 2 + n // 2 + 1)
                    act.activation(h1_hi[:, n, :], l1_out(n, last), ACT.Relu,
                                   bias=bias_1[:, n:n + 1]).then_inc(h1_split[0], 1)
                for m in range(N2):
                    act.wait_ge(l2_ready, i * 2 + m + 1)
                    act.activation(h2[:, m, :], ps_m[:, m, 0:SUPER], ACT.Relu,
                                   bias=bias_2[:, m:m + 1]).then_inc(h2_stored, 1)
                hot(2)
                act.wait_ge(l3_ready, i + 1)
                act.activation(y[:, bass.ds(i * HALVES, HALVES)], ps_m[:, 0, 0:HALVES],
                               ACT.Copy).then_inc(y_stored, 1)
                hot(3)

            def split_high(k):
                staged_w, hi, _ = weights[k]
                if k == 1:
                    act.wait_ge(wd_summed, 1)
                else:
                    act.wait_ge(weights_staged[k], 16)
                act.activation(hi[:], staged_w, ACT.Copy).then_inc(weights_hi, 1)

            act.memzero(y[:, :]).then_inc(y_stored, 1)
            for t in range(len(HOT)):
                act.wait_ge(table_loaded[t], 16)
                act.activation(hot_hi[:, t].rearrange("p c d -> p (c d)"), staged[:, t, :],
                               ACT.Copy).then_inc(hi_ready, 1)
            split_high(0)
            act.wait_ge(lo_ready, len(HOT))
            act.memzero(x[:, :, :, ROWS:PADDED]).then_inc(padding_cleared, 1)
            for a in range(HOT_BUFFERS // 2):
                store_hot(0, a)
            place_dense(0)
            act.wait_ge(small_weights_loaded, 3 * 16)
            supertile(0, True, False)
            with act.Fori(1, SUPERS - 1) as i:
                supertile(i, False, False)
            supertile(SUPERS - 1, False, True)

        @block.vector
        def _(dve):
            def split_low(t):
                dve.wait_ge(hi_ready, t + 1)
                dve.tensor_tensor(hot_lo[:, t].rearrange("p c d -> p (c d)"), staged[:, t, :],
                                  hot_hi[:, t].rearrange("p c d -> p (c d)").bitcast(f32),
                                  ALU.subtract).then_inc(lo_ready, 1)

            def split_low_weights(k):
                staged_w, hi, lo = weights[k]
                dve.wait_ge(weights_hi, k + 1)
                dve.tensor_tensor(lo[:], staged_w, hi[:].bitcast(f32), ALU.subtract).then_inc(weights_lo, 1)

            def make_onehot(i, t, first):
                if t >= HOT_BUFFERS:
                    dve.wait_ge(hot_read, i * len(HOT) + t - HOT_BUFFERS + 1)
                elif not first:
                    last_user = max(u for u in range(len(HOT)) if u % HOT_BUFFERS == t)
                    dve.wait_ge(hot_read, (i - 1) * len(HOT) + last_user + 1)
                for c in range(HOT_CHUNKS):
                    done = dve.tensor_scalar(onehot[:, t % HOT_BUFFERS, c, :], hot_index[0:HOT_ROWS, t, :],
                                             row_number[0:HOT_ROWS, c:c + 1], None, ALU.is_equal)
                done.then_inc(onehot_ready, 1)

            def supertile(i, first, last):
                def onehots(*ts):
                    if not last:
                        for t in ts:
                            make_onehot(i + 1, t, False)

                def next_ids():
                    if not last:
                        dve.wait_ge(hot_ids_loaded, (i + 2) * 16)

                def store_cold(banks):
                    for m in banks:
                        if m % 2:
                            dve.wait_ge(cold_turned, i * COLD_TURNS + m + 1)
                            dve.tensor_copy(*cold_store(m, last)).then_inc(stored_dve, 1)

                def split_dense():
                    dve.wait_ge(dense_split[0], i + 1)
                    dve.tensor_tensor(dense_lo[:, :], dense_rows[:, :], dense_hi[:, :].bitcast(f32),
                                      ALU.subtract).then_inc(dense_split[1], 1)

                if not first:
                    next_ids()
                    onehots(0)
                for h in range(HALVES):
                    store_cold(m for m in range(h * N_COLD, (h + 1) * N_COLD) if not (last and m in LATE_BANKS))
                    if first and h == 0:
                        for t in range(HOT_BUFFERS, len(HOT)):
                            make_onehot(0, t, True)
                        dve.wait_ge(weights_staged[1], 16)
                        dve.tensor_tensor(wd_staged[:, 0, :], wd_staged[:, 0, :], wd_staged[:, 1, :],
                                          ALU.add).then_inc(wd_summed, 1)
                        split_low_weights(0)
                        split_low_weights(1)
                        split_dense()
                        next_ids()
                        onehots(0, 1, 2)
                    elif h == 0:
                        split_dense()
                        onehots(1, 2, 3)
                if first:
                    split_low_weights(2)
                    onehots(3)
                onehots(4, 5)
                if last:
                    for c in range(GRAM_CHUNKS):
                        dve.wait_ge(gram_ready, i * GRAM_CHUNKS + c + 1)
                        for s in range(QUADS // 2, QUADS):
                            done = dve.tensor_copy(*gram_copy(c, s))
                        done.then_inc(gram_stored_dve, 1)
                        store_cold(m for m, after in LATE_BANKS.items() if after == c)
                if first:
                    dve.wait_ge(weights_lo, len(weights))
                for t in range(TURNS):
                    store_columns(dve, dve.tensor_copy, i, t, 0).then_inc(cols_stored[1], 1)
                for part in range(2):
                    dve.wait_ge(pairs_split[0], i * 2 + part + 1)
                    chunks = slice(0, 2) if part == 0 else slice(2, 3)
                    for c in range(PAIR_CHUNKS)[chunks]:
                        at = (c % 2) * SUPER
                        src = ps_m[0:CHUNK, part, at:at + SUPER].rearrange("p (s j) -> p s j", s=QUADS)
                        hi, lo = (v[:, c, :].rearrange("p (j s) -> p s j", s=QUADS) for v in (pairs_hi, pairs_lo))
                        done = dve.tensor_tensor(lo, src, hi.bitcast(f32), ALU.subtract)
                    done.then_inc(pairs_split[1], 1)
                onehots(*range(6, len(HOT)))
                for n in range(N1):
                    if last:
                        dve.wait_ge(h1_split[0], i * N1 + n + 1)
                    elif n % 2 == 0:
                        dve.wait_ge(h1_split[0], i * N1 + n + 2)
                    done = dve.tensor_scalar(h1[:, n, :], l1_out(n, last), bias_1[:, n:n + 1], 0.0, ALU.add, ALU.max)
                    if n % 2:
                        done.then_inc(h1_stored, 1)
                        dve.wait_ge(h1_stored, i * 2 + n // 2 + 1)
                        dve.tensor_tensor(h1_lo[:, n - 1:n + 1, :], h1[:, n - 1:n + 1, :],
                                          h1_hi[:, n - 1:n + 1, :].bitcast(f32),
                                          ALU.subtract).then_inc(h1_split[1], 1)
                dve.wait_ge(h2_stored, i * N2 + 1)
                dve.tensor_scalar(weighed[:, 0, :], h2[:, 0, :], w3_sb[:, 0:1], None,
                                  ALU.mult).then_inc(weighed_ready, 1)
                dve.wait_ge(h2_stored, (i + 1) * N2)
                dve.wait_ge(weighed_ready, i * N2 + 1)
                dve.scalar_tensor_tensor(weighed[:, 1, :], h2[:, 1, :], w3_sb[:, 1:2], weighed[:, 0, :],
                                         ALU.mult, ALU.add).then_inc(weighed_ready, 1)

            dve.memset(ones[:, :], 1.0).then_inc(ones_ready, 1)
            dve.memset(gram[:, :, :], 0.0).then_inc(padding_cleared, 1)
            dve.wait_ge(numbered, 1)
            dve.tensor_copy(row_number[:, :], row_number_int[:, :]).then_inc(row_number_ready, 1)
            dve.wait_ge(row_number_ready, 1)
            for t in range(len(HOT)):
                split_low(t)
                if t == 0:
                    dve.wait_ge(hot_ids_loaded, 16)
                if t < HOT_BUFFERS:
                    make_onehot(0, t, True)
            dve.wait_ge(lo_ready, len(HOT))
            dve.wait_ge(small_weights_loaded, 3 * 16)
            supertile(0, True, False)
            with dve.Fori(1, SUPERS - 1) as i:
                supertile(i, False, False)
            supertile(SUPERS - 1, False, True)

        @block.tensor
        def _(pe):
            def read_hot(i, t, first):
                if t % 2 == 0:
                    if t // 2 >= X_BANKS:
                        pe.wait_ge(stored_act, i * ACT_STORES + t // 2 - X_BANKS + 1)
                    elif not first:
                        last_user = max(a for a in range(N_HOT) if a % X_BANKS == t // 2)
                        pe.wait_ge(stored_act, (i - 1) * ACT_STORES + last_user + 1)
                if first:
                    pe.wait_ge(lo_ready, t + 1)
                pe.wait_ge(onehot_ready, i * len(HOT) + t + 1)
                o = ps[:, (t // 2) % X_BANKS, (t % 2) * SUPER:(t % 2 + 1) * SUPER]
                for c in range(HOT_CHUNKS):
                    for part in (hot_hi, hot_lo):
                        done = pe.matmul(o, part[:, t, c, :], onehot[:, t % HOT_BUFFERS, c, :],
                                         start=c == 0 and part is hot_hi,
                                         stop=c == HOT_CHUNKS - 1 and part is hot_lo)
                done.then_inc(hot_read, 1)

            def high_products(o, terms, start):
                for k, (w_hi, w_lo, z, _) in enumerate(terms):
                    pe.matmul(o, w_hi, z, start=start and k == 0, stop=False)
                    pe.matmul(o, w_lo, z, start=False, stop=False)

            def low_products(o, terms, stop=True):
                for k, (w_hi, _, _, z_lo) in enumerate(terms):
                    done = pe.matmul(o, w_hi, z_lo, start=False, stop=stop and k == len(terms) - 1)
                return done

            def dense_term(n):
                w = slice(n * 128, (n + 1) * 128)
                return [(wd_hi[:, w], wd_lo[:, w], dense_hi[:, :], dense_lo[:, :])]

            def pair_terms(n):
                w = slice(n * 128, (n + 1) * 128)
                return [(wp_hi[:, c, w], wp_lo[:, c, w], pairs_hi[:, c, :], pairs_lo[:, c, :])
                        for c in range(PAIR_CHUNKS)]

            def early_dense_products(n):
                high_products(l1_out(n, True), dense_term(n), True)
                low_products(l1_out(n, True), dense_term(n), False)

            def supertile(i, first, last):
                def hot(*ts):
                    if not last:
                        for t in ts:
                            read_hot(i + 1, t, False)

                def cold_in_x(m):
                    act_count, dve_count = cold_stored(m)
                    pe.wait_ge(stored_act, i * ACT_STORES + N_HOT + act_count)
                    pe.wait_ge(stored_dve, i * DVE_COLD + dve_count)

                def turn_cold(banks):
                    for m in banks:
                        h, b = divmod(m, N_COLD)
                        bank = cold_bank(m, last)
                        if h == 0 and bank == 2:
                            pe.wait_ge(y_stored, i + 1)
                        if h == 1 and not last and bank in (4, 6):
                            pe.wait_ge(gram_stored, i * GRAM_CHUNKS + HALF_CHUNKS - (bank == 4))
                        if h == 1 and last and b == 0:
                            pe.wait_ge(stored_act, i * ACT_STORES + N_HOT)
                        if h == 1 and last and bank == 3:
                            cold_in_x(N_COLD - 1)
                        pe.wait_ge(gathered[h][b], (i + 1) * gathers_of(b) * 16)
                        for k, slot in enumerate(COLD_BANKS[b]):
                            done = pe.transpose(ps[:, bank, k * 128:(k + 1) * 128], cold_rows[:, h, slot, :],
                                                ident[:, :])
                        done.then_inc(cold_turned, 1)

                turn_cold(range(N_COLD))
                if first:
                    for t in range(HOT_BUFFERS, len(HOT)):
                        read_hot(0, t, True)
                for h in range(HALVES):
                    if last and h == 0:
                        turn_cold(m for m in range(N_COLD, COLD_TURNS) if m not in LATE_BANKS)
                    if not last and h == 1:
                        turn_cold(range(N_COLD, COLD_TURNS))
                    if not (first and h == 0):
                        hot(h)
                    if first:
                        pe.wait_ge(padding_cleared, 2)
                    pe.wait_ge(dense_placed, i + 1)
                    cold_in_x((h + 1) * N_COLD - 1)
                    for c in range(h * HALF_CHUNKS, (h + 1) * HALF_CHUNKS):
                        if last and c == 1:
                            cold_in_x(min(LATE_BANKS) - 1)
                        if c % HALF_CHUNKS >= 2 or (last and h == 1):
                            pe.wait_ge(gram_stored, i * GRAM_CHUNKS + c - 1)
                            if last:
                                pe.wait_ge(gram_stored_dve, c - 1)
                        for q in range(GRAM_CHUNK):
                            j = c * GRAM_CHUNK + q
                            done = pe.matmul(ps_gram[0:STATIONARY, (c % 2) * GRAM_CHUNK + q, 0:QUADS * SIDE],
                                             x[:, j, :, :].rearrange("d s r -> d (s r)")[:, 1:1 + STATIONARY],
                                             x[:, j, :, 0:SIDE], start=True, stop=True)
                        done.then_inc(gram_ready, 1)
                        if last:
                            turn_cold(m for m, after in LATE_BANKS.items() if after == c)
                    if first and h == 0:
                        hot(0)
                hot(2)
                if last:
                    pe.wait_ge(dense_split[1], i + 1)
                    for n in (0, 2):
                        early_dense_products(n)
                pe.wait_ge(gram_stored, (i + 1) * GRAM_CHUNKS)
                if last:
                    pe.wait_ge(gram_stored_dve, GRAM_CHUNKS)
                pe.nop(nofuse=True)
                for t in range(TURNS):
                    for k, f in enumerate(columns_of(t)[::2]):
                        done = pe.transpose(ps[:, TURN_PS[t], k * 128:(k + 1) * 128],
                                            gram[:, f:f + 2, :].rearrange("q f j -> q (f j)"), ident[:, :])
                    done.then_inc(cols_turned, 1)
                hot(3)
                if last:
                    for n in (1, 3):
                        early_dense_products(n)
                pe.wait_ge(cols_stored[0], (i + 1) * TURNS)
                pe.wait_ge(cols_stored[1], (i + 1) * TURNS)
                pe.nop(nofuse=True)
                for c in range(PAIR_CHUNKS):
                    for s in range(QUADS):
                        at = (c % 2) * SUPER + s * GROUPS
                        done = pe.transpose(ps_m[0:CHUNK, c // 2, at:at + GROUPS],
                                            pairs[:, s, c * CHUNK:(c + 1) * CHUNK], ident[0:GROUPS, 0:GROUPS])
                    if c >= 1:
                        done.then_inc(pairs_turned, 1)
                hot(4)
                if first:
                    pe.wait_ge(weights_lo, len(weights))
                if not last:
                    pe.wait_ge(dense_split[1], i + 1)
                    pe.wait_ge(pairs_split[0], (i + 1) * 2)
                    pe.wait_ge(pairs_split[1], (i + 1) * 2)
                for n in range(N1):
                    o = l1_out(n, last)
                    if not last:
                        high_products(o, dense_term(n) + pair_terms(n), True)
                        done = low_products(o, dense_term(n) + pair_terms(n))
                    else:
                        if n == 0:
                            pe.wait_ge(pairs_split[0], i * 2 + 1)
                        high_products(o, pair_terms(n)[:2], False)
                        if n == 0:
                            pe.wait_ge(pairs_split[0], (i + 1) * 2)
                        high_products(o, pair_terms(n)[2:], False)
                        if n == 0:
                            pe.wait_ge(pairs_split[1], (i + 1) * 2)
                        done = low_products(o, pair_terms(n))
                    if n % 2:
                        done.then_inc(l1_ready, 1)
                hot(5)
                terms = [[(w2_hi[:, n, m * 128:(m + 1) * 128], w2_lo[:, n, m * 128:(m + 1) * 128],
                           h1_hi[:, n, :], h1_lo[:, n, :]) for n in range(N1)] for m in range(N2)]
                pe.wait_ge(h1_split[0], i * N1 + 2)
                if not last:
                    pe.wait_ge(h1_stored, i * 2 + 1)
                high_products(ps_m[:, 0, 0:SUPER], terms[0][:2], True)
                pe.wait_ge(h1_split[0], (i + 1) * N1)
                high_products(ps_m[:, 0, 0:SUPER], terms[0][2:], False)
                if not last:
                    pe.wait_ge(h1_stored, (i + 1) * 2)
                high_products(ps_m[:, 1, 0:SUPER], terms[1], True)
                pe.wait_ge(h1_split[1], (i + 1) * 2)
                for m in range(N2):
                    low_products(ps_m[:, m, 0:SUPER], terms[m]).then_inc(l2_ready, 1)
                hot(*range(6, len(HOT)))
                pe.wait_ge(h2_stored, (i + 1) * N2)
                pe.wait_ge(weighed_ready, (i + 1) * N2)
                for half in range(HALVES):
                    done = pe.matmul(ps_m[:, 0, half:half + 1], weighed[:, 1, half * 128:(half + 1) * 128],
                                     ones[:, :], start=True, stop=True)
                done.then_inc(l3_ready, 1)

            for t in range(HOT_BUFFERS):
                read_hot(0, t, True)
            pe.wait_ge(ident_ready, 1)
            pe.wait_ge(ones_ready, 1)
            supertile(0, True, False)
            with pe.Fori(1, SUPERS - 1) as i:
                supertile(i, False, False)
            supertile(SUPERS - 1, False, True)


def kernel(**inputs):
    import numpy as np
    import concourse.bacc as bacc
    from concourse.bass_utils import run_bass_kernel_spmd

    nc = bacc.Bacc("TRN2", target_bir_lowering=False, num_devices=1)
    arrays = {}

    def given(name, array):
        a = np.ascontiguousarray(array)
        arrays[name] = a
        return nc.dram_tensor(name, a.shape, mybir.dt.from_np(a.dtype), kind="ExternalInput").ap()

    def on_partitions(array, p):
        a = np.asarray(array)
        return a.reshape(-1, p, a.shape[-1]).transpose(1, 0, 2)

    all_ids = np.asarray(inputs["ids"])
    dense = given("dense_dram", np.asarray(inputs["r_dense_features"]).reshape(SUPERS, SUPER, DIM).transpose(0, 2, 1))
    ids = given("ids_dram", all_ids[:, COLD].reshape(SUPERS, HALVES, 128, len(COLD)).transpose(2, 1, 0, 3))
    hot_ids = given("hot_ids_dram", all_ids[:, HOT].reshape(SUPERS, SUPER, len(HOT))
                    .transpose(0, 2, 1).reshape(SUPERS, -1))
    tables = [given(f"tbl_{f}_dram", inputs[f"tbl_{f}"]) for f in range(FIELDS)]
    w1 = np.asarray(inputs["W_top1"])
    w_dense = given("w_dense_dram", on_partitions(np.concatenate([w1[:DIM], w1[DIM + PAIRS:]]), DIM))
    w_pairs = given("w_pairs_dram", on_partitions(w1[DIM:DIM + PAIRS][pair_order()], CHUNK))
    w_2 = given("w_2_dram", on_partitions(inputs["W_top2"], 128))
    w_3 = given("w_3_dram", np.asarray(inputs["W_top3"]).reshape(N2, 128).T)
    b1 = given("b1_dram", np.asarray(inputs["b_top1"]).reshape(N1, 128).T)
    b2 = given("b2_dram", np.asarray(inputs["b_top2"]).reshape(N2, 128).T)
    out = nc.dram_tensor("y_dram", (128, BATCH // 128), mybir.dt.float32, kind="ExternalOutput").ap()
    build(nc, dense, ids, hot_ids, tables, w_dense, w_pairs, w_2, b1, b2, w_3, out)
    result = run_bass_kernel_spmd(nc, [arrays], core_ids=[0])
    return result.results[0]["y_dram"].T.reshape(BATCH, 1)
```
